# Optimizing a Trainium2 kernel written in Bass

```python
import numpy as np
import jax
import jax.numpy as jnp

def _softmax(x, axis=-1):
    return jax.nn.softmax(x, axis=axis)

def _gelu(x):
    return jax.nn.gelu(x, approximate=True)

def _silu(x):
    return jax.nn.silu(x)

def _sigmoid(x):
    return jax.nn.sigmoid(x)

def _layernorm(x, axis=-1, eps=1e-05):
    m = jnp.mean(x, axis=axis, keepdims=True)
    v = jnp.var(x, axis=axis, keepdims=True)
    return (x - m) / jnp.sqrt(v + eps)

def _scatter_add(tgt, idx, src, axis=0):
    return tgt.at[idx].add(src)

def _segment_sum(src, seg, n):
    return jax.ops.segment_sum(src, seg, n)
kernel_name = 'mk_cond_resid_d1_seqx_r2_4b951d'

def setup_inputs(seed: int=0):
    np.random.seed(seed)
    _w = jnp.asarray

    def _rec_inputs():
        import jax
        import jax.numpy as jnp
        _rk = jax.random.key(seed)
        x = -7.109e-05 + 0.9999 * jax.random.normal(jax.random.fold_in(_rk, 1), (8, 512, 2048), jnp.float32)
        _lenS = 512 - jax.random.randint(jax.random.fold_in(_rk, 7), (8,), 0, max(1, 512 // 4) + 1, jnp.int32)
        _lenS2 = 512 - jax.random.randint(jax.random.fold_in(_rk, 8), (8,), 0, max(1, 512 // 4) + 1, jnp.int32)
        itok_B_0_15 = jax.random.randint(jax.random.fold_in(_rk, 11), (8,), 0, 16, jnp.int32)
        return (x, itok_B_0_15)
    x, itok_B_0_15 = _rec_inputs()

    def _L0_cond_setup():
        import jax, jax.numpy as jnp
        import numpy as np
        MAX_LORAS = 16
        IN, OUT = (2048, 2048)
        B, S = (8, 1024)
        key = jax.random.key(seed)
        k1, k2, k3 = jax.random.split(key, 3)
        x = jax.random.normal(k1, (B, S, IN), dtype=jnp.float32)
        adapter_ids = jax.random.randint(k2, (B,), 0, MAX_LORAS)
        weight = jax.random.normal(k3, (MAX_LORAS, OUT, IN), dtype=jnp.float32) * 0.02
        return {'x': x, 'adapter_ids': adapter_ids, 'weight': weight}
    _L0_cond_all = _L0_cond_setup()
    _L0_cond_in = {k: v for k, v in _L0_cond_all.items() if k in ('weight',)}
    del _L0_cond_all
    return {'x': x, 'itok_B_0_15': itok_B_0_15, 'L0_cond_weight': _L0_cond_in['weight']}

def reference(x, itok_B_0_15, L0_cond_weight):
    import jax
    import jax.numpy as jnp

    def _L0_cond_ref(x, adapter_ids, weight):
        import jax, jax.numpy as jnp
        import numpy as np
        MAX_LORAS = 16
        IN, OUT = (2048, 2048)
        B, S = (8, 1024)
        w = weight[adapter_ids]
        return jnp.einsum('bsi,boi->bso', x, w)
    x = x + _L0_cond_ref(x, itok_B_0_15, L0_cond_weight)
    return x

_drawn_inputs = setup_inputs


def setup_inputs(seed=0):
    import zlib

    import numpy as np

    out = dict(_drawn_inputs(seed))
    spreads = {}
    factors = {}
    for name, (base, spread) in spreads.items():
        noise = np.random.default_rng([zlib.crc32(name.encode()), seed]).standard_normal(out[name].shape)
        drawn = base * np.exp(spread * noise) if base else spread * noise
        out[name] = jnp.asarray(drawn.astype(out[name].dtype))
    for name, factor in factors.items():
        out[name] = (out[name] * factor).astype(out[name].dtype)
    return out
```

```python
import concourse.bass as bass
from concourse import mybir
from contextlib import ExitStack


def lora_residual_kernel(nc: bass.Bass, x_rows: bass.AP, x_cols: bass.AP, adapter_ids: bass.AP,
                         w_tiles: bass.AP, out: bass.AP):
    fp32 = mybir.dt.float32
    fp32r = mybir.dt.float32r
    ALU = mybir.AluOpType
    ACT = mybir.ActivationFunctionType

    P = 128
    BANK = 512
    B, S, D = x_rows.shape
    ADAPTERS, CHUNKS, KT, _, CW = w_tiles.shape
    MT = S // P
    HALVES = CW // BANK
    STEPS = CHUNKS * KT

    W_RAW = 8
    W_SPLIT = 4
    X_RAW = 4
    STORE_AT = W_RAW + W_SPLIT + 1
    LEAD = W_SPLIT - 1

    ctx = ExitStack()
    with ctx:
        def sb(name, shape, dt):
            return ctx.enter_context(nc.sbuf_tensor(name, shape, dt))

        def sem(name):
            return ctx.enter_context(nc.semaphore(name))

        ids = sb("ids", [1, B], mybir.dt.int32)
        w_raw = sb("w_raw", [P, W_RAW, CW], fp32)
        w_hi = sb("w_hi", [P, W_SPLIT, CW], fp32r)
        w_lo = sb("w_lo", [P, W_SPLIT, CW], fp32r)
        x_raw = sb("x_raw", [P, X_RAW, S], fp32)
        x_hi = sb("x_hi", [P, KT, S], fp32r)
        x_lo = sb("x_lo", [P, KT, S], fp32r)
        res = sb("res", [P, MT, CW], fp32)
        acc = ctx.enter_context(nc.psum_tensor("acc", [P, MT, CW], fp32))

        ids_loaded = sem("ids_loaded")
        w_loaded = [sem(f"w_loaded{i}") for i in range(W_RAW)]
        x_loaded = [sem(f"x_loaded{i}") for i in range(X_RAW)]
        res_loaded = [sem(f"res_loaded{m}") for m in range(MT)]
        stored = [sem(f"stored{m}") for m in range(MT)]
        w_hi_ready = sem("w_hi_ready")
        w_split = sem("w_split")
        x_hi_ready = sem("x_hi_ready")
        x_split = sem("x_split")
        step_done = sem("step_done")
        acc_done = sem("acc_done")
        acc_free = sem("acc_free")

        block = ctx.enter_context(nc.Block())

        @block.sync
        def _(sp):
            sp.dma_start(ids[:], adapter_ids).then_inc(ids_loaded, 16)
            sp.wait_ge(ids_loaded, 16)

            def load(b, steps):
                adapter = sp.value_load(ids[0:1, bass.ds(b, 1)], min_val=0, max_val=ADAPTERS - 1)
                for step in steps:
                    c, k = divmod(step, KT)
                    if c == 0:
                        sp.wait_ge(x_split, b * KT + k + 1)
                        sp.dma_start(x_raw[:, k % X_RAW, :],
                                     x_cols[bass.ds(b, 1), k, :, :].rearrange("o p s -> (o p) s")
                                     ).then_inc(x_loaded[k % X_RAW], 16)
                    sp.wait_ge(w_split, b * STEPS + step + 1)
                    sp.dma_start(w_raw[:, step % W_RAW, :],
                                 w_tiles[bass.ds(adapter, 1), c, k, :, :].rearrange("o p n -> (o p) n")
                                 ).then_inc(w_loaded[step % W_RAW], 16)

            def load_residual(b, c, m):
                sp.dma_start(res[:, m, :], x_rows[bass.ds(b, 1), m * P:(m + 1) * P, c * CW:(c + 1) * CW]
                             .rearrange("o p n -> (o p) n")).then_inc(res_loaded[m], 16)

            def store(b, c):
                sp.wait_ge(acc_free, (b * CHUNKS + c + 2) * MT)
                for m in reversed(range(MT)):
                    sp.dma_start(out[bass.ds(b, 1), m * P:(m + 1) * P, c * CW:(c + 1) * CW]
                                 .rearrange("o p n -> (o p) n"), res[:, m, :]).then_inc(stored[m], 16)

            load(0, range(KT - 1))
            for m in range(MT):
                load_residual(0, 0, m)
            with sp.Fori(0, B - 1) as b:
                for c in range(CHUNKS):
                    load(b, [c * KT + KT - 1])
                    if c < CHUNKS - 1:
                        load(b, range((c + 1) * KT, (c + 1) * KT + STORE_AT))
                        store(b, c)
                        load(b, range((c + 1) * KT + STORE_AT, (c + 2) * KT - 1))
                    else:
                        load(b + 1, range(STORE_AT))
                        store(b, c)
                        load(b + 1, range(STORE_AT, KT - 1))
                    for m in range(MT):
                        sp.wait_ge(stored[m], (b * CHUNKS + c + 1) * 16)
                        load_residual(b + (c + 1) // CHUNKS, (c + 1) % CHUNKS, m)
            for c in range(CHUNKS):
                load(B - 1, [c * KT + KT - 1])
                if c < CHUNKS - 1:
                    load(B - 1, range((c + 1) * KT, (c + 1) * KT + STORE_AT))
                    store(B - 1, c)
                    load(B - 1, range((c + 1) * KT + STORE_AT, (c + 2) * KT - 1))
                    for m in range(MT):
                        sp.wait_ge(stored[m], ((B - 1) * CHUNKS + c + 1) * 16)
                        load_residual(B - 1, c + 1, m)
                else:
                    for m in range(MT):
                        sp.wait_ge(acc_free, (B * CHUNKS) * MT + m + 1)
                        sp.dma_start(out[B - 1, m * P:(m + 1) * P, c * CW:(c + 1) * CW],
                                     res[:, m, :]).then_inc(stored[m], 16)
            for m in range(MT):
                sp.wait_ge(stored[m], B * CHUNKS * 16)

        @block.scalar
        def _(act):
            with act.Fori(0, B) as b:
                for step in range(STEPS):
                    k = step % KT
                    if step < KT:
                        act.wait_ge(x_loaded[k % X_RAW], (b * (KT // X_RAW) + k // X_RAW) * 16 + 16)
                        act.wait_ge(step_done, b * STEPS + step + 1)
                        nc.scalar.activation(x_hi[:, k, :], x_raw[:, k % X_RAW, :],
                                             ACT.Copy).then_inc(x_hi_ready, 1)
                    act.wait_ge(w_loaded[step % W_RAW], (b * (STEPS // W_RAW) + step // W_RAW) * 16 + 16)
                    act.wait_ge(step_done, b * STEPS + step + 1)
                    nc.scalar.activation(w_hi[:, step % W_SPLIT, :], w_raw[:, step % W_RAW, :],
                                         ACT.Copy).then_inc(w_hi_ready, 1)

        @block.vector
        def _(dve):
            def split_w(b, step):
                dve.wait_ge(w_hi_ready, b * STEPS + step + 1)
                nc.vector.tensor_tensor(w_lo[:, step % W_SPLIT, :], w_raw[:, step % W_RAW, :],
                                        w_hi[:, step % W_SPLIT, :].bitcast(fp32),
                                        ALU.subtract).then_inc(w_split, 1)

            def split(b, steps):
                for step in steps:
                    if step < KT:
                        dve.wait_ge(x_hi_ready, b * KT + step + 1)
                        nc.vector.tensor_tensor(x_lo[:, step, :], x_raw[:, step % X_RAW, :],
                                                x_hi[:, step, :].bitcast(fp32),
                                                ALU.subtract).then_inc(x_split, 1)
                    split_w(b, step)

            def empty(b, c):
                for m in range(MT):
                    dve.wait_ge(res_loaded[m], (b * CHUNKS + c) * 16 + 16)
                    if m < MT - 1:
                        dve.wait_ge(acc_done, (b * CHUNKS + c) * (MT - 1) + m + 1)
                    else:
                        dve.wait_ge(step_done, b * STEPS + (c + 1) * KT + W_SPLIT)
                    nc.vector.tensor_tensor(res[:, m, :], acc[:, m, :], res[:, m, :],
                                            ALU.add).then_inc(acc_free, 1)

            dve.sem_inc(w_split, W_RAW)
            dve.sem_inc(x_split, X_RAW)
            split(0, range(LEAD))
            with dve.Fori(0, B - 1) as b:
                for c in range(CHUNKS):
                    split(b, range(c * KT + LEAD, min((c + 1) * KT + LEAD, STEPS)))
                    if c == CHUNKS - 1:
                        split(b + 1, range(LEAD))
                    empty(b, c)
            for c in range(CHUNKS):
                split(B - 1, range(c * KT + LEAD, min((c + 1) * KT + LEAD, STEPS)))
                empty(B - 1, c)

        @block.tensor
        def _(pe):
            pe.sem_inc(step_done, W_SPLIT)
            pe.sem_inc(acc_free, MT)
            with pe.Fori(0, B) as b:
                for step in range(STEPS):
                    c, k = divmod(step, KT)
                    if c == 0:
                        pe.wait_ge(x_split, b * KT + k + 1 + X_RAW)
                    pe.wait_ge(w_split, b * STEPS + step + 1 + W_RAW)
                    for m in range(MT):
                        if k == 0:
                            pe.wait_ge(acc_free, (b * CHUNKS + c) * MT + m + 1)
                        xh = x_hi[:, k, m * P:(m + 1) * P]
                        xl = x_lo[:, k, m * P:(m + 1) * P]
                        terms = [(xh, w_hi), (xh, w_lo), (xl, w_hi)]
                        for n, (xs, ws) in enumerate(terms):
                            for h in range(HALVES):
                                cols = slice(h * BANK, (h + 1) * BANK)
                                last = nc.tensor.matmul(acc[:, m, cols], xs, ws[:, step % W_SPLIT, cols],
                                                        start=(k == 0 and n == 0),
                                                        stop=(k == KT - 1 and n == len(terms) - 1))
                        if k == KT - 1 and m < MT - 1:
                            last.then_inc(acc_done, 1)
                    last.then_inc(step_done, 1)


def kernel(**inputs):
    import numpy as np
    import concourse.bacc as bacc
    from concourse.bass_utils import run_bass_kernel_spmd

    x = np.ascontiguousarray(inputs["x"])
    ids = np.ascontiguousarray(inputs["itok_B_0_15"]).reshape(1, -1)
    weight = np.asarray(inputs["L0_cond_weight"])
    B, S, D = x.shape
    ADAPTERS, OUT, _ = weight.shape
    P, CHUNKS = 128, 2

    x_cols = np.ascontiguousarray(x.transpose(0, 2, 1)).reshape(B, D // P, P, S)
    w_tiles = np.ascontiguousarray(
        weight.reshape(ADAPTERS, CHUNKS, OUT // CHUNKS, D // P, P).transpose(0, 1, 3, 4, 2))

    nc = bacc.Bacc("TRN2", target_bir_lowering=False, num_devices=1)
    arrays = {"x_rows": x, "x_cols": x_cols, "adapter_ids": ids, "w_tiles": w_tiles}
    args = [nc.dram_tensor(name, a.shape, mybir.dt.from_np(a.dtype), kind="ExternalInput").ap()
            for name, a in arrays.items()]
    out = nc.dram_tensor("out", x.shape, mybir.dt.float32, kind="ExternalOutput").ap()
    lora_residual_kernel(nc, *args, out)
    ran = run_bass_kernel_spmd(nc, [arrays], core_ids=[0])
    return ran.results[0]["out"]
```

```python
import concourse.bass as bass
from concourse import mybir
from contextlib import ExitStack


def lora_residual_kernel(nc: bass.Bass, x_rows: bass.AP, x_cols: bass.AP, adapter_ids: bass.AP,
                         w_tiles: bass.AP, out: bass.AP):
    fp32 = mybir.dt.float32
    fp32r = mybir.dt.float32r
    ALU = mybir.AluOpType
    ACT = mybir.ActivationFunctionType

    P = 128
    BANK = 512
    B, S, D = x_rows.shape
    ADAPTERS, CHUNKS, KT, _, CW = w_tiles.shape
    MT = S // P
    HALVES = CW // BANK
    STEPS = CHUNKS * KT

    W_RAW = 8
    W_SPLIT = 4
    X_RAW = 4
    STORE_AT = W_RAW + W_SPLIT + 1
    PIECES = STEPS + HALVES - 1
    PARTS = MT + HALVES - 1
    WARM_UP = 14
    LAST = 2
    LEAD = W_SPLIT - LAST

    ctx = ExitStack()
    with ctx:
        def sb(name, shape, dt):
            return ctx.enter_context(nc.sbuf_tensor(name, shape, dt))

        def sem(name):
            return ctx.enter_context(nc.semaphore(name))

        ids = sb("ids", [1, B], mybir.dt.int32)
        w_raw = sb("w_raw", [P, W_RAW, CW], fp32)
        w_hi = sb("w_hi", [P, W_SPLIT, CW], fp32r)
        w_lo = sb("w_lo", [P, W_SPLIT, CW], fp32r)
        x_raw = sb("x_raw", [P, X_RAW, S], fp32)
        x_hi = sb("x_hi", [P, KT, S], fp32r)
        x_lo = sb("x_lo", [P, KT, S], fp32r)
        zeros = sb("zeros", [P, BANK], mybir.dt.bfloat16)
        table_load = sb("table_load", [P, 1], fp32)
        res = sb("res", [P, MT, CW], fp32)
        acc = ctx.enter_context(nc.psum_tensor("acc", [P, MT, CW], fp32))

        ids_loaded = sem("ids_loaded")
        w_loaded = [sem(f"w_loaded{i}") for i in range(W_RAW)]
        first_loaded = [sem(f"first_loaded{h}") for h in range(HALVES - 1)]
        x_loaded = [sem(f"x_loaded{i}") for i in range(X_RAW)]
        res_loaded = [sem(f"res_loaded{m}") for m in range(MT)]
        stored = [sem(f"stored{m}") for m in range(MT)]
        w_hi_ready = sem("w_hi_ready")
        w_split = sem("w_split")
        x_hi_ready = sem("x_hi_ready")
        x_split = sem("x_split")
        step_done = sem("step_done")
        acc_done = sem("acc_done")
        acc_free = sem("acc_free")
        zeros_ready = sem("zeros_ready")
        last_stored = [sem(f"last_stored{h}") for h in range(HALVES - 1)]

        def half(h):
            return slice(h * BANK, (h + 1) * BANK)

        def pieces(step):
            return [half(h) for h in range(HALVES)] if step == 0 else [slice(0, CW)]

        def split_by(b, step):
            return b * PIECES + step + HALVES

        block = ctx.enter_context(nc.Block())

        @block.sync
        def _(sp):
            sp.dma_start(ids[:], adapter_ids).then_inc(ids_loaded, 16)
            sp.dma_start(x_raw[:, 0, :], x_cols[0, 0, :, :]).then_inc(x_loaded[0], 16)
            sp.wait_ge(ids_loaded, 16)

            def load(b, steps, x_ahead=0):
                adapter = sp.value_load(ids[0:1, bass.ds(b, 1)], min_val=0, max_val=ADAPTERS - 1)
                for step in steps:
                    c, k = divmod(step, KT)
                    if c == 0 and k >= x_ahead:
                        sp.wait_ge(x_split, b * KT + k + 1)
                        sp.dma_start(x_raw[:, k % X_RAW, :],
                                     x_cols[bass.ds(b, 1), k, :, :].rearrange("o p s -> (o p) s")
                                     ).then_inc(x_loaded[k % X_RAW], 16)
                    if step < W_RAW:
                        sp.wait_ge(w_split, b * PIECES + step + 1)
                    else:
                        sp.wait_ge(w_split, split_by(b, step))
                    loaded = [*first_loaded, w_loaded[0]] if step == 0 else [w_loaded[step % W_RAW]]
                    for cols, signal in zip(pieces(step), loaded):
                        sp.dma_start(w_raw[:, step % W_RAW, cols],
                                     w_tiles[bass.ds(adapter, 1), c, k, :, cols]
                                     .rearrange("o p n -> (o p) n")).then_inc(signal, 16)

            def load_residual(b, c, m):
                sp.dma_start(res[:, m, :], x_rows[bass.ds(b, 1), m * P:(m + 1) * P, c * CW:(c + 1) * CW]
                             .rearrange("o p n -> (o p) n")).then_inc(res_loaded[m], 16)

            def store(b, c):
                sp.wait_ge(acc_free, (b * CHUNKS + c + 2) * PARTS)
                for m in reversed(range(MT)):
                    sp.dma_start(out[bass.ds(b, 1), m * P:(m + 1) * P, c * CW:(c + 1) * CW]
                                 .rearrange("o p n -> (o p) n"), res[:, m, :]).then_inc(stored[m], 16)

            load(0, range(KT - 1), x_ahead=1)
            for m in range(MT):
                load_residual(0, 0, m)
            with sp.Fori(0, B - 1) as b:
                for c in range(CHUNKS):
                    load(b, [c * KT + KT - 1])
                    if c < CHUNKS - 1:
                        load(b, range((c + 1) * KT, (c + 1) * KT + STORE_AT))
                        store(b, c)
                        load(b, range((c + 1) * KT + STORE_AT, (c + 2) * KT - 1))
                    else:
                        load(b + 1, range(STORE_AT))
                        store(b, c)
                        load(b + 1, range(STORE_AT, KT - 1))
                    for m in range(MT):
                        sp.wait_ge(stored[m], (b * CHUNKS + c + 1) * 16)
                        load_residual(b + (c + 1) // CHUNKS, (c + 1) % CHUNKS, m)
            for c in range(CHUNKS):
                load(B - 1, [c * KT + KT - 1])
                if c < CHUNKS - 1:
                    load(B - 1, range((c + 1) * KT, (c + 1) * KT + STORE_AT))
                    store(B - 1, c)
                    load(B - 1, range((c + 1) * KT + STORE_AT, (c + 2) * KT - 1))
                    for m in range(MT):
                        sp.wait_ge(stored[m], ((B - 1) * CHUNKS + c + 1) * 16)
                        load_residual(B - 1, c + 1, m)
                else:
                    tiles = [(m, slice(0, CW)) for m in range(MT - 1)]
                    tiles += [(MT - 1, half(h)) for h in range(HALVES)]
                    for n, (m, cols) in enumerate(tiles):
                        sp.wait_ge(acc_free, B * CHUNKS * PARTS + n + 1)
                        sp.dma_start(out[B - 1, m * P:(m + 1) * P, c * CW + cols.start:c * CW + cols.stop],
                                     res[:, m, cols]
                                     ).then_inc(([*stored, *last_stored])[n], 16)
            for m in range(MT):
                sp.wait_ge(stored[m], B * CHUNKS * 16)
            for signal in last_stored:
                sp.wait_ge(signal, 16)

        @block.scalar
        def _(act):
            act.wait_ge(zeros_ready, 1)
            nc.scalar.activation(table_load[:], zeros[:, 0:1], ACT.Copy)
            with act.Fori(0, B) as b:
                for step in range(STEPS):
                    k = step % KT
                    act.wait_ge(step_done, b * STEPS + step + 1)
                    if step < KT:
                        act.wait_ge(x_loaded[k % X_RAW], (b * (KT // X_RAW) + k // X_RAW) * 16 + 16)
                        nc.scalar.activation(x_hi[:, k, :], x_raw[:, k % X_RAW, :],
                                             ACT.Copy).then_inc(x_hi_ready, 1)
                    for n, cols in enumerate(pieces(step)):
                        if n < len(pieces(step)) - 1:
                            act.wait_ge(first_loaded[n], b * 16 + 16)
                        else:
                            act.wait_ge(w_loaded[step % W_RAW], (b * (STEPS // W_RAW) + step // W_RAW) * 16 + 16)
                        nc.scalar.activation(w_hi[:, step % W_SPLIT, cols], w_raw[:, step % W_RAW, cols],
                                             ACT.Copy).then_inc(w_hi_ready, 1)

        @block.vector
        def _(dve):
            def split_w(b, step):
                for n, cols in enumerate(pieces(step)):
                    dve.wait_ge(w_hi_ready, split_by(b, step) - len(pieces(step)) + n + 1)
                    nc.vector.tensor_tensor(w_lo[:, step % W_SPLIT, cols], w_raw[:, step % W_RAW, cols],
                                            w_hi[:, step % W_SPLIT, cols].bitcast(fp32),
                                            ALU.subtract).then_inc(w_split, 1)

            def split(b, steps):
                for step in steps:
                    if step < KT:
                        dve.wait_ge(x_hi_ready, b * KT + step + 1)
                        nc.vector.tensor_tensor(x_lo[:, step, :], x_raw[:, step % X_RAW, :],
                                                x_hi[:, step, :].bitcast(fp32),
                                                ALU.subtract).then_inc(x_split, 1)
                    split_w(b, step)

            def empty(b, c):
                for m in range(MT):
                    dve.wait_ge(res_loaded[m], (b * CHUNKS + c) * 16 + 16)
                    for h in range(HALVES if m == MT - 1 else 1):
                        cols = half(h) if m == MT - 1 else slice(0, CW)
                        if m + h < PARTS - 1:
                            dve.wait_ge(acc_done, (b * CHUNKS + c) * (PARTS - 1) + m + h + 1)
                        else:
                            dve.wait_ge(step_done, b * STEPS + (c + 1) * KT + W_SPLIT)
                        nc.vector.tensor_tensor(res[:, m, cols], acc[:, m, cols], res[:, m, cols],
                                                ALU.add).then_inc(acc_free, 1)

            nc.vector.memset(zeros[:], 0.0).then_inc(zeros_ready, 1)
            dve.sem_inc(w_split, W_RAW)
            dve.sem_inc(x_split, X_RAW)
            split(0, range(LEAD))
            with dve.Fori(0, B - 1) as b:
                for c in range(CHUNKS):
                    split(b, range(c * KT + LEAD, min((c + 1) * KT + LEAD, STEPS)))
                    if c == CHUNKS - 1:
                        split(b + 1, range(LEAD))
                    empty(b, c)
            for c in range(CHUNKS):
                split(B - 1, range(c * KT + LEAD, min((c + 1) * KT + LEAD, STEPS)))
                empty(B - 1, c)

        @block.tensor
        def _(pe):
            pe.sem_inc(step_done, W_SPLIT)
            pe.sem_inc(acc_free, PARTS)
            pe.wait_ge(zeros_ready, 1)
            for n in range(WARM_UP):
                nc.tensor.matmul(acc[:, 0, 0:BANK], zeros[:, 0:P], zeros[:], start=True, stop=True)

            def products(step, m, halves):
                k = step % KT
                xh = x_hi[:, k, m * P:(m + 1) * P]
                xl = x_lo[:, k, m * P:(m + 1) * P]
                terms = [(xh, w_hi), (xh, w_lo), (xl, w_hi)]
                for n, (xs, ws) in enumerate(terms):
                    for h in halves:
                        last = nc.tensor.matmul(acc[:, m, half(h)], xs, ws[:, step % W_SPLIT, half(h)],
                                                start=(k == 0 and n == 0),
                                                stop=(k == KT - 1 and n == len(terms) - 1))
                return last

            with pe.Fori(0, B) as b:
                for c in range(CHUNKS):
                    for k in range(KT - LAST):
                        step = c * KT + k
                        if c == 0:
                            pe.wait_ge(x_split, b * KT + k + 1 + X_RAW)
                        if step == 0:
                            for h in range(HALVES):
                                pe.wait_ge(w_split, b * PIECES + h + 1 + W_RAW)
                                for m in range(MT):
                                    if h == 0 or m == MT - 1:
                                        pe.wait_ge(acc_free, b * CHUNKS * PARTS + m + h + 1)
                                    last = products(step, m, [h])
                        else:
                            pe.wait_ge(w_split, split_by(b, step) + W_RAW)
                            for m in range(MT):
                                if k == 0:
                                    emptied = PARTS if m == MT - 1 else m + 1
                                    pe.wait_ge(acc_free, (b * CHUNKS + c) * PARTS + emptied)
                                last = products(step, m, range(HALVES))
                        last.then_inc(step_done, 1)
                    end = (c + 1) * KT - 1
                    if c == 0:
                        pe.wait_ge(x_split, (b + 1) * KT + X_RAW)
                    pe.wait_ge(w_split, split_by(b, end) + W_RAW)
                    for m in range(MT):
                        for step in range(end - LAST + 1, end):
                            last = products(step, m, range(HALVES))
                            if m == MT - 1:
                                last.then_inc(step_done, 1)
                        if m < MT - 1:
                            products(end, m, range(HALVES)).then_inc(acc_done, 1)
                        else:
                            for h in range(HALVES - 1):
                                products(end, m, [h]).then_inc(acc_done, 1)
                            products(end, m, [HALVES - 1]).then_inc(step_done, 1)


def kernel(**inputs):
    import numpy as np
    import concourse.bacc as bacc
    from concourse.bass_utils import run_bass_kernel_spmd

    x = np.ascontiguousarray(inputs["x"])
    ids = np.ascontiguousarray(inputs["itok_B_0_15"]).reshape(1, -1)
    weight = np.asarray(inputs["L0_cond_weight"])
    B, S, D = x.shape
    ADAPTERS, OUT, _ = weight.shape
    P, CHUNKS = 128, 2

    x_cols = np.ascontiguousarray(x.transpose(0, 2, 1)).reshape(B, D // P, P, S)
    w_tiles = np.ascontiguousarray(
        weight.reshape(ADAPTERS, CHUNKS, OUT // CHUNKS, D // P, P).transpose(0, 1, 3, 4, 2))

    nc = bacc.Bacc("TRN2", target_bir_lowering=False, num_devices=1)
    arrays = {"x_rows": x, "x_cols": x_cols, "adapter_ids": ids, "w_tiles": w_tiles}
    args = [nc.dram_tensor(name, a.shape, mybir.dt.from_np(a.dtype), kind="ExternalInput").ap()
            for name, a in arrays.items()]
    out = nc.dram_tensor("out", x.shape, mybir.dt.float32, kind="ExternalOutput").ap()
    lora_residual_kernel(nc, *args, out)
    ran = run_bass_kernel_spmd(nc, [arrays], core_ids=[0])
    return ran.results[0]["out"]
```
